# Optimizing a Trainium2 kernel written in Bass

```python
import numpy as np
import jax
import jax.numpy as jnp

def _softmax(x, axis=-1):
    return jax.nn.softmax(x, axis=axis)

def _gelu(x):
    return jax.nn.gelu(x, approximate=True)

def _silu(x):
    return jax.nn.silu(x)

def _sigmoid(x):
    return jax.nn.sigmoid(x)

def _layernorm(x, axis=-1, eps=1e-05):
    m = jnp.mean(x, axis=axis, keepdims=True)
    v = jnp.var(x, axis=axis, keepdims=True)
    return (x - m) / jnp.sqrt(v + eps)

def _scatter_add(tgt, idx, src, axis=0):
    return tgt.at[idx].add(src)

def _segment_sum(src, seg, n):
    return jax.ops.segment_sum(src, seg, n)
kernel_name = 'mk_recurrent_d1_jaxref_r4_c5611c'

def setup_inputs(seed: int=0):
    np.random.seed(seed)
    _w = jnp.asarray

    def _L0_attn_setup():
        import jax, jax.numpy as jnp
        import numpy as np
        EMBED_DIM = 256
        NUM_HEADS = 16
        HEAD_DIM = EMBED_DIM // NUM_HEADS
        ROPE_BASE = 10000.0

        def _rotary_emb(seq_len, dtype=jnp.float32):
            half = HEAD_DIM // 2
            inv_freq = 1.0 / ROPE_BASE ** (jnp.arange(half, dtype=dtype) / half)
            pos = jnp.arange(seq_len, dtype=dtype)
            sinusoid = pos[:, None] * inv_freq[None, :]
            sin = jnp.sin(sinusoid)
            cos = jnp.cos(sinusoid)
            sin = jnp.stack((sin, sin), axis=-1).reshape(seq_len, HEAD_DIM)
            cos = jnp.stack((cos, cos), axis=-1).reshape(seq_len, HEAD_DIM)
            return (sin, cos)

        def _rotate_half(x):
            x1 = x[..., ::2]
            x2 = x[..., 1::2]
            return jnp.stack((-x2, x1), axis=-1).reshape(x.shape)

        def _apply_rope(x, sin, cos):
            return x * cos[None, None] + _rotate_half(x) * sin[None, None]
        key = jax.random.key(seed)
        ks = jax.random.split(key, 9)
        B, S, E = (2, 512, EMBED_DIM)
        scale = 1.0 / np.sqrt(E)
        x = jax.random.normal(ks[0], (B, S, E), dtype=jnp.float32)
        Wq = jax.random.normal(ks[1], (E, E), dtype=jnp.float32) * scale
        bq = jnp.zeros((E,), dtype=jnp.float32)
        Wk = jax.random.normal(ks[2], (E, E), dtype=jnp.float32) * scale
        bk = jnp.zeros((E,), dtype=jnp.float32)
        Wv = jax.random.normal(ks[3], (E, E), dtype=jnp.float32) * scale
        bv = jnp.zeros((E,), dtype=jnp.float32)
        Wo = jax.random.normal(ks[4], (E, E), dtype=jnp.float32) * scale
        bo = jnp.zeros((E,), dtype=jnp.float32)
        return {'x': x, 'Wq': Wq, 'bq': bq, 'Wk': Wk, 'bk': bk, 'Wv': Wv, 'bv': bv, 'Wo': Wo, 'bo': bo}
    _L0_attn_in = _L0_attn_setup()

    def _L0_ffn_setup():
        import jax, jax.numpy as jnp
        import numpy as np
        DIM = 256
        DEPTH = 2
        HEADS = 8
        DIM_HEAD = 64
        WINDOW = 128
        INNER = HEADS * DIM_HEAD
        HID = int(DIM * 4 * 2 / 3)
        B, N = (2, 2048)
        QK_SCALE = 8.0

        def shift_token(t):
            t1, t2 = jnp.split(t, 2, axis=-1)
            t2 = jnp.pad(t2, ((0, 0), (1, 0), (0, 0)))[:, :-1]
            return jnp.concatenate([t1, t2], axis=-1)

        def l2norm(t):
            return t / jnp.clip(jnp.linalg.norm(t, axis=-1, keepdims=True), 1e-12)

        def rotate_half(x):
            x1, x2 = jnp.split(x, 2, axis=-1)
            return jnp.concatenate([-x2, x1], axis=-1)

        def rotary_xpos(q, k):
            n = q.shape[-2]
            half_idx = jnp.arange(0, DIM_HEAD, 2, dtype=jnp.float32)
            inv_freq = 1.0 / 10000.0 ** (half_idx / DIM_HEAD)
            t = jnp.arange(n, dtype=jnp.float32)
            freqs = t[:, None] * inv_freq[None, :]
            freqs = jnp.concatenate([freqs, freqs], axis=-1)
            base = (half_idx + 0.4 * DIM_HEAD) / (1.4 * DIM_HEAD)
            power = (t - n // 2) / float(WINDOW // 2)
            scale = base[None, :] ** power[:, None]
            scale = jnp.concatenate([scale, scale], axis=-1)
            cos, sin = (jnp.cos(freqs), jnp.sin(freqs))
            q = q * cos * scale + rotate_half(q) * sin * scale
            k = k * cos / scale + rotate_half(k) * sin / scale
            return (q, k)

        def local_attention(q, k, v):
            b, h, n, d = q.shape
            w = n // WINDOW
            bq = q.reshape(b, h, w, WINDOW, d) * QK_SCALE
            bk = k.reshape(b, h, w, WINDOW, d)
            bv = v.reshape(b, h, w, WINDOW, d)

            def look_around(t):
                p = jnp.pad(t, ((0, 0), (0, 0), (1, 0), (0, 0), (0, 0)))
                return jnp.concatenate([p[:, :, :w], p[:, :, 1:]], axis=3)
            bk, bv = (look_around(bk), look_around(bv))
            bt = jnp.arange(n).reshape(w, WINDOW)
            btp = jnp.pad(bt, ((1, 0), (0, 0)), constant_values=-1)
            btk = jnp.concatenate([btp[:w], btp[1:]], axis=1)
            sim = jnp.einsum('bhwid,bhwjd->bhwij', bq, bk)
            i = bt[:, :, None]
            j = btk[:, None, :]
            mask = (i < j) | (i > j + WINDOW) | (j == -1)
            sim = jnp.where(mask, -jnp.finfo(sim.dtype).max, sim)
            attn = jax.nn.softmax(sim, axis=-1)
            out = jnp.einsum('bhwij,bhwjd->bhwid', attn, bv)
            return out.reshape(b, h, n, d)

        def _layer(x, wqkv, qs, ksc, wo, lg, lb, w1, b1, w2, b2):
            b, n, _ = x.shape
            h = shift_token(x)
            qkv = h @ wqkv
            q, k, v = jnp.split(qkv, 3, axis=-1)
            to_heads = lambda t: t.reshape(b, n, HEADS, DIM_HEAD).transpose(0, 2, 1, 3)
            q, k, v = (to_heads(q), to_heads(k), to_heads(v))
            q = l2norm(q) * qs
            k = l2norm(k) * ksc
            q, k = rotary_xpos(q, k)
            o = local_attention(q, k, v)
            o = o.transpose(0, 2, 1, 3).reshape(b, n, INNER)
            x = x + o @ wo
            h = shift_token(x)
            mu = h.mean(-1, keepdims=True)
            var = h.var(-1, keepdims=True)
            h = (h - mu) / jnp.sqrt(var + 1e-05) * lg + lb
            h = h @ w1 + b1
            a, g = jnp.split(h, 2, axis=-1)
            h = a * jax.nn.gelu(g, approximate=False)
            x = x + h @ w2 + b2
            return x
        key = jax.random.key(seed)
        ks = jax.random.split(key, 6)
        return {'x': jax.random.normal(ks[0], (B, N, DIM), jnp.float32), 'wqkv': jax.random.normal(ks[1], (DEPTH, DIM, 3 * INNER), jnp.float32) * 0.02, 'q_scale': jnp.ones((DEPTH, DIM_HEAD), jnp.float32), 'k_scale': jnp.ones((DEPTH, DIM_HEAD), jnp.float32), 'wo': jax.random.normal(ks[2], (DEPTH, INNER, DIM), jnp.float32) * 0.02, 'ln_g': jnp.ones((DEPTH, DIM), jnp.float32), 'ln_b': jnp.zeros((DEPTH, DIM), jnp.float32), 'w1': jax.random.normal(ks[3], (DEPTH, DIM, 2 * HID), jnp.float32) * 0.02, 'b1': jnp.zeros((DEPTH, 2 * HID), jnp.float32), 'w2': jax.random.normal(ks[4], (DEPTH, HID, DIM), jnp.float32) * 0.02, 'b2': jnp.zeros((DEPTH, DIM), jnp.float32)}
    _L0_ffn_in = _L0_ffn_setup()
    _d = {'L0_attn_x': _L0_attn_in['x'], 'L0_attn_Wq': _L0_attn_in['Wq'], 'L0_attn_bq': _L0_attn_in['bq'], 'L0_attn_Wk': _L0_attn_in['Wk'], 'L0_attn_bk': _L0_attn_in['bk'], 'L0_attn_Wv': _L0_attn_in['Wv'], 'L0_attn_bv': _L0_attn_in['bv'], 'L0_attn_Wo': _L0_attn_in['Wo'], 'L0_attn_bo': _L0_attn_in['bo'], 'L0_ffn_wqkv': _L0_ffn_in['wqkv'], 'L0_ffn_q_scale': _L0_ffn_in['q_scale'], 'L0_ffn_k_scale': _L0_ffn_in['k_scale'], 'L0_ffn_wo': _L0_ffn_in['wo'], 'L0_ffn_ln_g': _L0_ffn_in['ln_g'], 'L0_ffn_ln_b': _L0_ffn_in['ln_b'], 'L0_ffn_w1': _L0_ffn_in['w1'], 'L0_ffn_b1': _L0_ffn_in['b1'], 'L0_ffn_w2': _L0_ffn_in['w2'], 'L0_ffn_b2': _L0_ffn_in['b2']}
    _x0 = _d['L0_attn_x']
    _d['L0_attn_x'] = jax.random.normal(jax.random.fold_in(jax.random.key(seed), 1), (1, 4096, 256), dtype=_x0.dtype)
    del _x0
    return _d

def reference(L0_attn_x, L0_attn_Wq, L0_attn_bq, L0_attn_Wk, L0_attn_bk, L0_attn_Wv, L0_attn_bv, L0_attn_Wo, L0_attn_bo, L0_ffn_wqkv, L0_ffn_q_scale, L0_ffn_k_scale, L0_ffn_wo, L0_ffn_ln_g, L0_ffn_ln_b, L0_ffn_w1, L0_ffn_b1, L0_ffn_w2, L0_ffn_b2):

    def _L0_attn_ref(x, Wq, bq, Wk, bk, Wv, bv, Wo, bo):
        import jax, jax.numpy as jnp
        import numpy as np
        EMBED_DIM = 256
        NUM_HEADS = 16
        HEAD_DIM = EMBED_DIM // NUM_HEADS
        ROPE_BASE = 10000.0

        def _rotary_emb(seq_len, dtype=jnp.float32):
            half = HEAD_DIM // 2
            inv_freq = 1.0 / ROPE_BASE ** (jnp.arange(half, dtype=dtype) / half)
            pos = jnp.arange(seq_len, dtype=dtype)
            sinusoid = pos[:, None] * inv_freq[None, :]
            sin = jnp.sin(sinusoid)
            cos = jnp.cos(sinusoid)
            sin = jnp.stack((sin, sin), axis=-1).reshape(seq_len, HEAD_DIM)
            cos = jnp.stack((cos, cos), axis=-1).reshape(seq_len, HEAD_DIM)
            return (sin, cos)

        def _rotate_half(x):
            x1 = x[..., ::2]
            x2 = x[..., 1::2]
            return jnp.stack((-x2, x1), axis=-1).reshape(x.shape)

        def _apply_rope(x, sin, cos):
            return x * cos[None, None] + _rotate_half(x) * sin[None, None]
        B, S, E = x.shape
        H, D = (NUM_HEADS, HEAD_DIM)

        def proj(W, b):
            t = x @ W.T + b
            return t.reshape(B, S, H, D).transpose(0, 2, 1, 3)
        q = proj(Wq, bq)
        k = proj(Wk, bk)
        v = proj(Wv, bv)
        sin, cos = _rotary_emb(S, x.dtype)
        q = _apply_rope(q, sin, cos)
        k = _apply_rope(k, sin, cos)
        scores = jnp.einsum('bhqd,bhkd->bhqk', q, k) / jnp.sqrt(jnp.asarray(D, x.dtype))
        causal = jnp.tril(jnp.ones((S, S), dtype=bool))
        scores = jnp.where(causal[None, None], scores, -jnp.inf)
        weights = jax.nn.softmax(scores, axis=-1)
        out = jnp.einsum('bhqk,bhkd->bhqd', weights, v)
        out = out.transpose(0, 2, 1, 3).reshape(B, S, E)
        return out @ Wo.T + bo

    def _L0_ffn_ref(x, wqkv, q_scale, k_scale, wo, ln_g, ln_b, w1, b1, w2, b2):
        import jax, jax.numpy as jnp
        import numpy as np
        DIM = 256
        DEPTH = 2
        HEADS = 8
        DIM_HEAD = 64
        WINDOW = 128
        INNER = HEADS * DIM_HEAD
        HID = int(DIM * 4 * 2 / 3)
        B, N = (2, 2048)
        QK_SCALE = 8.0

        def shift_token(t):
            t1, t2 = jnp.split(t, 2, axis=-1)
            t2 = jnp.pad(t2, ((0, 0), (1, 0), (0, 0)))[:, :-1]
            return jnp.concatenate([t1, t2], axis=-1)

        def l2norm(t):
            return t / jnp.clip(jnp.linalg.norm(t, axis=-1, keepdims=True), 1e-12)

        def rotate_half(x):
            x1, x2 = jnp.split(x, 2, axis=-1)
            return jnp.concatenate([-x2, x1], axis=-1)

        def rotary_xpos(q, k):
            n = q.shape[-2]
            half_idx = jnp.arange(0, DIM_HEAD, 2, dtype=jnp.float32)
            inv_freq = 1.0 / 10000.0 ** (half_idx / DIM_HEAD)
            t = jnp.arange(n, dtype=jnp.float32)
            freqs = t[:, None] * inv_freq[None, :]
            freqs = jnp.concatenate([freqs, freqs], axis=-1)
            base = (half_idx + 0.4 * DIM_HEAD) / (1.4 * DIM_HEAD)
            power = (t - n // 2) / float(WINDOW // 2)
            scale = base[None, :] ** power[:, None]
            scale = jnp.concatenate([scale, scale], axis=-1)
            cos, sin = (jnp.cos(freqs), jnp.sin(freqs))
            q = q * cos * scale + rotate_half(q) * sin * scale
            k = k * cos / scale + rotate_half(k) * sin / scale
            return (q, k)

        def local_attention(q, k, v):
            b, h, n, d = q.shape
            w = n // WINDOW
            bq = q.reshape(b, h, w, WINDOW, d) * QK_SCALE
            bk = k.reshape(b, h, w, WINDOW, d)
            bv = v.reshape(b, h, w, WINDOW, d)

            def look_around(t):
                p = jnp.pad(t, ((0, 0), (0, 0), (1, 0), (0, 0), (0, 0)))
                return jnp.concatenate([p[:, :, :w], p[:, :, 1:]], axis=3)
            bk, bv = (look_around(bk), look_around(bv))
            bt = jnp.arange(n).reshape(w, WINDOW)
            btp = jnp.pad(bt, ((1, 0), (0, 0)), constant_values=-1)
            btk = jnp.concatenate([btp[:w], btp[1:]], axis=1)
            sim = jnp.einsum('bhwid,bhwjd->bhwij', bq, bk)
            i = bt[:, :, None]
            j = btk[:, None, :]
            mask = (i < j) | (i > j + WINDOW) | (j == -1)
            sim = jnp.where(mask, -jnp.finfo(sim.dtype).max, sim)
            attn = jax.nn.softmax(sim, axis=-1)
            out = jnp.einsum('bhwij,bhwjd->bhwid', attn, bv)
            return out.reshape(b, h, n, d)

        def _layer(x, wqkv, qs, ksc, wo, lg, lb, w1, b1, w2, b2):
            b, n, _ = x.shape
            h = shift_token(x)
            qkv = h @ wqkv
            q, k, v = jnp.split(qkv, 3, axis=-1)
            to_heads = lambda t: t.reshape(b, n, HEADS, DIM_HEAD).transpose(0, 2, 1, 3)
            q, k, v = (to_heads(q), to_heads(k), to_heads(v))
            q = l2norm(q) * qs
            k = l2norm(k) * ksc
            q, k = rotary_xpos(q, k)
            o = local_attention(q, k, v)
            o = o.transpose(0, 2, 1, 3).reshape(b, n, INNER)
            x = x + o @ wo
            h = shift_token(x)
            mu = h.mean(-1, keepdims=True)
            var = h.var(-1, keepdims=True)
            h = (h - mu) / jnp.sqrt(var + 1e-05) * lg + lb
            h = h @ w1 + b1
            a, g = jnp.split(h, 2, axis=-1)
            h = a * jax.nn.gelu(g, approximate=False)
            x = x + h @ w2 + b2
            return x
        for l in range(DEPTH):
            x = _layer(x, wqkv[l], q_scale[l], k_scale[l], wo[l], ln_g[l], ln_b[l], w1[l], b1[l], w2[l], b2[l])
        return x
    x = L0_attn_x
    xn = _layernorm(x, axis=-1)
    s = _L0_attn_ref(xn, L0_attn_Wq, L0_attn_bq, L0_attn_Wk, L0_attn_bk, L0_attn_Wv, L0_attn_bv, L0_attn_Wo, L0_attn_bo)
    g = _silu(_L0_ffn_ref(xn, L0_ffn_wqkv, L0_ffn_q_scale, L0_ffn_k_scale, L0_ffn_wo, L0_ffn_ln_g, L0_ffn_ln_b, L0_ffn_w1, L0_ffn_b1, L0_ffn_w2, L0_ffn_b2))
    x = x + s * g
    return x

_drawn_inputs = setup_inputs


def setup_inputs(seed=0):
    import zlib

    import numpy as np

    out = dict(_drawn_inputs(seed))
    spreads = {'L0_attn_bq': (0.0, 0.8),
     'L0_attn_bk': (0.0, 0.8),
     'L0_attn_bv': (0.0, 0.1),
     'L0_attn_bo': (0.0, 0.1),
     'L0_ffn_q_scale': (1.0, 0.6),
     'L0_ffn_k_scale': (1.0, 0.6),
     'L0_ffn_ln_g': (1.0, 0.6),
     'L0_ffn_ln_b': (0.0, 0.8),
     'L0_ffn_b1': (0.0, 0.8),
     'L0_ffn_b2': (0.0, 2.0)}
    factors = {'L0_ffn_wqkv': 8.0, 'L0_ffn_wo': 8.0, 'L0_ffn_w1': 8.0, 'L0_ffn_w2': 8.0}
    for name, (base, spread) in spreads.items():
        noise = np.random.default_rng([zlib.crc32(name.encode()), seed]).standard_normal(out[name].shape)
        drawn = base * np.exp(spread * noise) if base else spread * noise
        out[name] = jnp.asarray(drawn.astype(out[name].dtype))
    for name, factor in factors.items():
        out[name] = (out[name] * factor).astype(out[name].dtype)
    return out
```

```python
from contextlib import ExitStack, contextmanager

import concourse.bass as bass
from concourse import mybir

F32 = mybir.dt.float32
BF16 = mybir.dt.bfloat16
F32R = mybir.dt.float32r
ALU = mybir.AluOpType
ACT = mybir.ActivationFunctionType
AX = mybir.AxisListType

P = 128
S = 4096
E = 256
NT = S // P
C = 512
NC = S // C
TPC = C // P
EC = E // P
EPS = 1e-5
MASKED = -1e30

H, D = 16, 16
GH = 4
G = H // GH
DV = D + 1
NPART = 3
K_TERMS = (0, 1, 2, 0, 1, 0)
Q_TERMS = (0, 0, 0, 1, 1, 2)
KQ = len(K_TERMS) * D
KM = KQ + NPART

LH, LD = 8, 64
INNER = LH * LD
DEPTH = 2
HID = E * 4 * 2 // 3
HC = (HID + P - 1) // P
HP = HC * P


def repeat(eng, n, body):
    body(0)
    with eng.Fori(1, n) as c:
        body(c)


def upto(eng, s, n):
    if not isinstance(n, int) or n > 0:
        eng.wait_ge(s, n)


@contextmanager
def semaphores(nc, prefix=""):
    taken = []

    def sem(name):
        taken.append(nc.alloc_semaphore(prefix + name))
        return taken[-1]

    yield sem
    nc.clear_and_free_semaphores(taken)
    nc.all_engine_barrier()


def layer_norm_and_project(nc, ctx0, X, x, w_qkv, b_cols, b_v, cos, sin, ident, k_parts, q_parts, v_aug):
    with ExitStack() as ctx:
        def sb(name, shape, dt=F32):
            return ctx.enter_context(nc.sbuf_tensor(name, shape, dt))

        sem = ctx.enter_context(semaphores(nc))

        w_sb = sb("pw", [P, EC, 5 * E])
        bc_sb = sb("pbc", [P, 8])
        bv_sb = sb("pbv", [P, E])
        id_sb = sb("pid", [P, P])
        cos_sb = sb("pcos", [P, S])
        sin_sb = sb("psin", [P, S])
        stats = sb("pstats", [P, TPC, 6])
        mv = sb("pmv", [P, NT, 2])
        ve = sb("pve", [P, NT])
        half = sb("phalf", [P, TPC])
        rstd = sb("prstd", [P, NT])
        xs = sb("pxs", [P, TPC, E])
        xT = sb("pxT", [P, EC, C])
        ta = sb("pta", [P, 2, C])
        tb = sb("ptb", [P, 2, C])
        rot = sb("prot", [P, 2, C])
        rest = sb("prest", [P, 2, C])
        parts = sb("pparts", [P, 2, NPART, C], BF16)
        v_sb = sb("pvsb", [P, TPC, H, DV])
        ps_t = ctx.enter_context(nc.psum_tensor("pps_t", [P, EC, C], F32))
        ps_p = ctx.enter_context(nc.psum_tensor("pps_p", [P, 2, 2, C], F32))
        ps_v = ctx.enter_context(nc.psum_tensor("pps_v", [P, TPC, E], F32))

        x_in = [sem(f"p_x_in{i}") for i in range(NC)]
        w_in = sem("p_w_in")
        stat_done = sem("p_stat_done")
        aggr_done = sem("p_aggr_done")
        half_set = sem("p_half_set")
        pool_ve = sem("p_pool_ve")
        rstd_done = sem("p_rstd_done")
        xn_done = sem("p_xn_done")
        xs_done = sem("p_xs_done")
        t_done = sem("p_t_done")
        xT_done = sem("p_xT_done")
        p_done = sem("p_p_done")
        v_done = sem("p_v_done")
        rope_done = sem("p_rope_done")
        vsb_done = sem("p_vsb_done")
        ones_set = sem("p_ones_set")
        rot_done = sem("p_rot_done")
        p1_done = sem("p_p1_done")
        rest_done = sem("p_rest_done")
        p2_done = sem("p_p2_done")
        p3_done = sem("p_p3_done")
        parts_out = [sem(f"p_parts_out{i}") for i in range(2)]
        v_out = sem("p_v_out")
        NG = 4

        block = ctx.enter_context(nc.Block())

        @block.sync
        def _(sp):
            for c in range(NC):
                sp.dma_start(X[:, c * TPC:(c + 1) * TPC, :],
                             x[c * C:(c + 1) * C, :].rearrange("(a p) e -> p a e", p=P)).then_inc(x_in[c], 16)
                if c == 0:
                    for dst, src in ((w_sb[:, :, :], w_qkv), (bc_sb[:, :], b_cols), (bv_sb[:, :], b_v),
                                     (id_sb[:, :], ident), (cos_sb[:, :], cos), (sin_sb[:, :], sin)):
                        sp.dma_start(dst, src).then_inc(w_in, 16)
            def chunk(c):
                token, tile = (c * C, c * TPC) if isinstance(c, int) else (sp.snap(c * C), sp.snap(c * TPC))
                for g in range(NG):
                    sp.wait_ge(p3_done, c * NG + g + 1)
                    dst = (q_parts, k_parts)[g // 2]
                    r = g % 2
                    for t in range(NPART):
                        sp.dma_start(dst[8 * r:8 * r + 8, t, :, bass.ds(token, C)],
                                     parts[:, g % 2, t, :]).then_inc(parts_out[g % 2], 16)
                sp.wait_ge(vsb_done, c + 1)
                for g in range(G):
                    sp.dma_start(v_aug[g, :, bass.ds(tile, TPC), :],
                                 v_sb[:, :, GH * g:GH * g + GH, :].rearrange("p a h d -> p a (h d)")
                                 ).then_inc(v_out, 16)
            repeat(sp, NC, chunk)
            for i in range(2):
                sp.wait_ge(parts_out[i], 16 * NPART * 2 * NC)
            sp.wait_ge(v_out, 16 * G * NC)

        @block.gpsimd
        def _(pool):
            pool.memset(half[:, :], -0.5).then_inc(half_set, 1)
            pool.wait_ge(half_set, 1)
            for c in range(NC):
                pool.wait_ge(aggr_done, c * TPC + TPC)
                pool.tensor_scalar(ve[:, c * TPC:(c + 1) * TPC], mv[:, c * TPC:(c + 1) * TPC, 1], EPS, None, ALU.add).then_inc(pool_ve, 1)
                pool.wait_ge(pool_ve, c + 1)
                pool.tensor_tensor(rstd[:, c * TPC:(c + 1) * TPC], ve[:, c * TPC:(c + 1) * TPC], half[:, :], ALU.pow).then_inc(rstd_done, 1)
            def chunk(c):
                for g in range(NG):
                    n = c * NG + g
                    b = g % 2
                    pool.wait_ge(rope_done, 2 * n + 2)
                    pool.tensor_tensor(rot[:, b, :], ta[:, b, :], tb[:, b, :], ALU.add).then_inc(rot_done, 1)
                    pool.wait_ge(rot_done, n + 1)
                    pool.wait_ge(p1_done, n + 1)
                    pool.tensor_tensor(rest[:, b, :], rot[:, b, :], parts[:, b, 0, :], ALU.subtract).then_inc(rest_done, 1)
                    pool.wait_ge(rest_done, n + 1)
                    pool.wait_ge(p2_done, n + 1)
                    pool.tensor_tensor(parts[:, b, 2, :], rest[:, b, :], parts[:, b, 1, :], ALU.subtract).then_inc(p3_done, 1)
            repeat(pool, NC, chunk)

        @block.scalar
        def _(act):
            def chunk(c):
                act.wait_ge(xn_done, c * TPC + TPC)
                upto(act, t_done, c)
                act.activation(xs[:, :, :], X[:, bass.ds(c * TPC, TPC), :], ACT.Copy).then_inc(xs_done, 1)
                act.wait_ge(t_done, c + 1)
                upto(act, v_done, c)
                act.activation(xT[:, :, :], ps_t[:, :, :], ACT.Copy).then_inc(xT_done, 1)
                for g in range(NG):
                    n = c * NG + g
                    b = g % 2
                    act.wait_ge(rot_done, n + 1)
                    upto(act, parts_out[b], 16 * NPART * (c * 2 + g // 2))
                    act.activation(parts[:, b, 0, :], rot[:, b, :], ACT.Copy).then_inc(p1_done, 1)
                    act.wait_ge(rest_done, n + 1)
                    act.activation(parts[:, b, 1, :], rest[:, b, :], ACT.Copy).then_inc(p2_done, 1)
            repeat(act, NC, chunk)

        @block.tensor
        def _(pe):
            pe.wait_ge(w_in, 6 * 16)
            def chunk(c):
                pe.wait_ge(xs_done, c + 1)
                upto(pe, xT_done, c)
                for a in range(TPC):
                    for e in range(EC):
                        last = pe.transpose(ps_t[:, e, a * P:(a + 1) * P], xs[:, a, e * P:(e + 1) * P], id_sb[:, :])
                last.then_inc(t_done, 1)
                pe.wait_ge(xT_done, c + 1)
                for g in range(NG):
                    n = c * NG + g
                    upto(pe, rope_done, c * (2 * NG) + max(0, 2 * (g - 1)))
                    col = (g // 2) * 2 * E + (g % 2) * P
                    for s in range(2):
                        for e in range(EC):
                            last = pe.matmul(ps_p[:, g % 2, s, :], w_sb[:, e, col + s * E:col + s * E + P], xT[:, e, :],
                                             start=(e == 0), stop=(e == EC - 1))
                    last.then_inc(p_done, 1)
                upto(pe, vsb_done, c)
                for a in range(TPC):
                    for e in range(EC):
                        last = pe.matmul(ps_v[:, a, :], xT[:, e, a * P:(a + 1) * P], w_sb[:, e, 4 * E:5 * E],
                                         start=(e == 0), stop=(e == EC - 1))
                last.then_inc(v_done, 1)
            repeat(pe, NC, chunk)

        @block.vector
        def _(dve):
            dve.memset(v_sb[:, :, :, D:DV], 1.0).then_inc(ones_set, 1)
            for c in range(NC):
                dve.wait_ge(x_in[c], 16)
                for a in range(TPC):
                    if c > 0 and a == 0:
                        dve.wait_ge(aggr_done, c * TPC)
                    dve.bn_stats(stats[:, a, :], X[:, c * TPC + a, :]).then_inc(stat_done, 1)
                for a in range(TPC):
                    dve.wait_ge(stat_done, c * TPC + a + 1)
                    dve.bn_aggr(mv[:, c * TPC + a, :], stats[:, a, :]).then_inc(aggr_done, 1)
            dve.wait_ge(aggr_done, NT)
            for c in range(NC):
                dve.wait_ge(rstd_done, c + 1)
                for a in range(TPC):
                    t = c * TPC + a
                    dve.tensor_scalar(X[:, t, :], X[:, t, :], mv[:, t, 0:1], rstd[:, t:t + 1],
                                      ALU.subtract, ALU.mult).then_inc(xn_done, 1)
            dve.wait_ge(w_in, 6 * 16)
            dve.wait_ge(ones_set, 1)
            def chunk(c):
                for g in range(NG):
                    n = c * NG + g
                    b = g % 2
                    dve.wait_ge(p_done, n + 1)
                    upto(dve, rot_done, c * NG + max(0, g - 1))
                    j = (g // 2) * 4 + g % 2
                    dve.scalar_tensor_tensor(out=ta[:, b, :], in0=ps_p[:, b, 0, :], scalar=bc_sb[:, j:j + 1],
                                             in1=cos_sb[:, bass.ds(c * C, C)], op0=ALU.add, op1=ALU.mult
                                             ).then_inc(rope_done, 1)
                    dve.scalar_tensor_tensor(out=tb[:, b, :], in0=ps_p[:, b, 1, :], scalar=bc_sb[:, j + 2:j + 3],
                                             in1=sin_sb[:, bass.ds(c * C, C)], op0=ALU.add, op1=ALU.mult
                                             ).then_inc(rope_done, 1)
                dve.wait_ge(v_done, c + 1)
                upto(dve, v_out, 16 * G * c)
                for a in range(TPC):
                    last = dve.tensor_tensor(v_sb[:, a, :, 0:D], ps_v[:, a, :].rearrange("p (h d) -> p h d", d=D),
                                             bv_sb[:, :].rearrange("p (h d) -> p h d", d=D), ALU.add)
                last.then_inc(vsb_done, 1)
            repeat(dve, NC, chunk)


def pace(order):
    AHEAD = 3
    units = []
    for b, (half, j) in enumerate(order):
        units.append([("max", b, a, h, cc) for a in range(TPC) for h in range(GH) for cc in range(j + 1)])
    steps = []
    flat, marks = [], []
    for b in range(len(order)):
        flat += units[b]
        marks.append(len(flat))
    sent = marks[0]
    turned = 0
    plan = []
    for b, (half, j) in enumerate(order):
        n = TPC * (j + 1)
        for i in range(n):
            t = i + 1 + AHEAD
            want = marks[b]
            if b + 1 < len(order):
                size = marks[b + 1] - marks[b]
                want += min(size, size * t // n)
                if t > n and b + 2 < len(order):
                    n2 = TPC * (order[b + 1][1] + 1)
                    want += min(marks[b + 2] - marks[b + 1], (marks[b + 2] - marks[b + 1]) * (t - n) // n2)
            turn = [("turn", m) for m in range(turned + 1, len(order)) if marks[m] <= sent]
            turned += len(turn)
            new = flat[sent:max(sent, want)]
            sent = max(sent, want)
            plan.append((b, half, j, i, turn, new))
    return units[0] + [("turn", 0)], plan


def global_attention(nc, k_parts, q_parts, v_aug, o_raw, identb, mask_k, mask_q, ones):
    with ExitStack() as ctx:
        def sb(name, shape, dt=F32):
            return ctx.enter_context(nc.sbuf_tensor(name, shape, dt))

        sem = ctx.enter_context(semaphores(nc))

        QR, MR, SR, PR = 3, 3, 2, 3
        kst = [sb(f"kst{i}", [KM, GH, S], BF16) for i in range(2)]
        qst = [sb(f"qst{i}", [KM, GH, C], BF16) for i in range(QR)]
        vst = [sb(f"vst{i}", [P, NT, GH * DV]) for i in range(2)]
        probs = sb("probs", [P, PR, GH, C])
        mp = [sb(f"mp{i}", [P, TPC * GH, NC]) for i in range(2)]
        negm = sb("negm", [P, 2, TPC * GH])
        mrest = sb("mrest", [P, 2, TPC * GH])
        zero = sb("mzero", [P, TPC * GH])
        msplit = sb("msplit", [P, 2, TPC * GH, NPART], BF16)
        mrow = sb("mrow", [GH * NPART, 2, C], BF16)
        o_sb = sb("o_sb", [P, 2, C])
        id_b = sb("id_b", [P, P], BF16)
        mk_sb = sb("mk_sb", [P, P], BF16)
        mq_sb = sb("mq_sb", [P, P], BF16)
        ps_s = [ctx.enter_context(nc.psum_tensor(f"ps_s{i}", [P, 2, C], F32)) for i in range(SR)]
        ps_m = [ctx.enter_context(nc.psum_tensor(f"ps_m{i}", [P, C], F32)) for i in range(MR)]
        ps_o = ctx.enter_context(nc.psum_tensor("ps_o", [P, C], F32))

        const_in = sem("g_const_in")
        zero_set = sem("g_zero_set")
        k_in = [[sem(f"g_k_in{h}_{j}") for j in range(NC)] for h in range(2)]
        q_in = [sem(f"g_q_in{i}") for i in range(QR)]
        m_in = [sem(f"g_m_in{i}") for i in range(QR)]
        max_scored = sem("g_max_scored")
        max_read = sem("g_max_read")
        negm_done = sem("g_negm_done")
        m1_done = sem("g_m1_done")
        m2_done = sem("g_m2_done")
        mr_done = sem("g_mr_done")
        split_done = sem("g_split_done")
        scored = sem("g_scored")
        exp_done = sem("g_exp_done")
        pv_done = sem("g_pv_done")
        o_done = sem("g_o_done")
        o_out = [sem(f"g_o_out{i}") for i in range(2)]
        o_zero = sem("g_o_zero")
        turns_clear = sem("g_turns_clear")

        ITS = G // 2
        order = [(0, j) for j in range(NC)] + [(1, j) for j in reversed(range(NC))]
        NB = len(order)
        first, plan = pace(order)
        NSTEP = len(plan)
        NMAX = sum(TPC * GH * (j + 1) for _, j in order)
        NUNIT = NMAX + NB
        last_step = {}
        for s, st in enumerate(plan):
            last_step[st[0]] = s
        unit_at, max_last = {}, {}
        u = nm = 0
        for unit in first + [x for st in plan for x in st[4] + st[5]]:
            unit_at[unit] = u
            u += 1
            if unit[0] == "max":
                nm += 1
                max_last[unit[1]] = u
        assert u == NUNIT and nm == NMAX

        def turn_at(b):
            return unit_at[("turn", b)] + 1

        def q_slot(b):
            return b % QR

        def q_uses(b):
            return b // QR, len([x for x in range(NB) if x % QR == b % QR])

        block = ctx.enter_context(nc.Block())

        @block.sync
        def _(sp):
            for dst, src in ((id_b, identb), (mk_sb, mask_k), (mq_sb, mask_q)):
                sp.dma_start(dst[:, :], src).then_inc(const_in, 16)
            for i in range(2):
                sp.dma_start(kst[i][KQ:KM, :, :], ones).then_inc(const_in, 16)
            with sp.Fori(0, ITS) as it:
                group = [sp.snap(it * 2), sp.snap(it * 2 + 1)]
                head = [sp.snap(it * 2 * GH), sp.snap(it * 2 * GH + GH)]

                def load_k(half, j):
                    cols = slice(j * C, (j + 1) * C)
                    kh = k_parts[bass.ds(head[half], GH), :, :, cols]
                    for lo, hi, n in ((0, 48, 3), (48, 80, 2), (80, 96, 1)):
                        sp.dma_start(kst[half][lo:hi, :, cols],
                                     kh[:, 0:n].rearrange("h t d n -> (t d) h n")).then_inc(k_in[half][j], 16)
                    sp.dma_start(vst[half][:, j * TPC:(j + 1) * TPC, :],
                                 v_aug[bass.ds(group[half], 1), :, j * TPC:(j + 1) * TPC, :].rearrange("g p a n -> (g p) a n")
                                 ).then_inc(k_in[half][j], 16)

                def load_q(b):
                    half, j = order[b]
                    for r, t in enumerate(Q_TERMS):
                        sp.dma_start(qst[q_slot(b)][r * D:(r + 1) * D, :, :],
                                     q_parts[bass.ds(head[half], GH), t, :, j * C:(j + 1) * C].rearrange("h d n -> d h n")
                                     ).then_inc(q_in[q_slot(b)], 16)

                sp.wait_ge(turns_clear, it + 1)
                load_k(0, 0)
                load_q(0)
                load_k(0, 1)
                load_q(1)
                load_q(2)
                for j in range(2, NC):
                    load_k(0, j)
                for j in range(NC):
                    load_k(1, j)
                for b in range(NB):
                    sp.wait_ge(max_read, it * NUNIT + turn_at(b))
                    for h in range(GH):
                        sp.dma_start(qst[q_slot(b)][KQ:KM, h, :], mrow[NPART * h:NPART * h + NPART, b % 2, :]
                                     ).then_inc(m_in[q_slot(b)], 16)
                    if b >= 1:
                        sp.wait_ge(o_done, it * NB + b)
                        sp.dma_start(o_raw[bass.ds(group[order[b - 1][0]], 1), order[b - 1][1], :, :].rearrange("g p n -> (g p) n"),
                                     o_sb[:, (b - 1) % 2, :]).then_inc(o_out[(b - 1) % 2], 16)
                        if b + 2 < NB:
                            load_q(b + 2)
            sp.wait_ge(turns_clear, ITS + 1)

        @block.gpsimd
        def _(pool):
            pool.memset(zero[:, :], 0.0).then_inc(zero_set, 1)
            pool.wait_ge(zero_set, 1)
            with pool.Fori(0, ITS) as it:
                for b in range(NB):
                    n = it * NB + b
                    p = b % 2
                    pool.wait_ge(negm_done, n + 1)
                    if b >= 2:
                        pool.wait_ge(max_scored, it * NUNIT + turn_at(b - 2))
                    pool.tensor_tensor(msplit[:, p, :, 0], negm[:, p, :], zero[:, :], ALU.add).then_inc(m1_done, 1)
                    pool.wait_ge(m1_done, n + 1)
                    pool.tensor_tensor(mrest[:, p, :], negm[:, p, :], msplit[:, p, :, 0], ALU.subtract).then_inc(mr_done, 1)
                    pool.wait_ge(mr_done, n + 1)
                    pool.tensor_tensor(msplit[:, p, :, 1], mrest[:, p, :], zero[:, :], ALU.add).then_inc(m2_done, 1)
                    pool.wait_ge(m2_done, n + 1)
                    pool.tensor_tensor(msplit[:, p, :, 2], mrest[:, p, :], msplit[:, p, :, 1], ALU.subtract).then_inc(split_done, 1)

        @block.scalar
        def _(act):
            def take_sums(it, b):
                act.wait_ge(pv_done, it * NSTEP + last_step[b] + 1)
                if b >= 2:
                    act.wait_ge(o_out[b % 2], 16 * (it * (NB // 2) + b // 2))
                act.activation(o_sb[:, b % 2, :], ps_o[:, :], ACT.Copy).then_inc(o_done, 1)

            act.sem_inc(turns_clear, 1)
            with act.Fori(0, ITS) as it:
                for s, (b, half, j, i, _, _) in enumerate(plan):
                    off = max(0, i - TPC * j) * P
                    if s >= PR:
                        act.wait_ge(pv_done, it * NSTEP + (s - PR + 1))
                    for hp in range(2):
                        act.wait_ge(scored, it * (2 * NSTEP) + 2 * s + hp + 1)
                        act.activation(probs[:, s % PR, 2 * hp:2 * hp + 2, off:C], ps_s[hp][:, :, off:C], ACT.Exp,
                                       scale=float(D) ** -0.5).then_inc(exp_done, 1)
                    if i == 0 and b > 0:
                        take_sums(it, b - 1)
                take_sums(it, NB - 1)
                act.wait_ge(o_done, it * NB + NB)
                act.dma_start(o_raw[bass.ds(it * 2 + order[NB - 1][0], 1), order[NB - 1][1], :, :].rearrange("g p n -> (g p) n"),
                              o_sb[:, (NB - 1) % 2, :]).then_inc(o_out[(NB - 1) % 2], 16)
                act.wait_ge(pv_done, it * NSTEP + NSTEP)
                for i in range(2):
                    act.wait_ge(o_out[i], (it + 1) * (16 * (NB // 2)))
                act.sem_inc(turns_clear, 1)

        @block.vector
        def _(dve):
            dve.memset(ps_o[:, :], 0.0).then_inc(o_zero, 1)
            with dve.Fori(0, ITS) as it:
                def do(unit):
                    b = unit[1]
                    half, j = order[b]
                    n = unit_at[unit]
                    bank = ps_m[n % MR]
                    if unit[0] == "max":
                        _, _, a, h, cc = unit
                        width = P * (a + 1) if cc == j else C
                        dve.wait_ge(max_scored, it * NUNIT + n + 1)
                        dve.tensor_reduce(mp[b % 2][:, a * GH + h, cc:cc + 1], bank[:, 0:width], AX.X, ALU.max
                                          ).then_inc(max_read, 1)
                        if n + 1 == max_last[b]:
                            dve.wait_ge(max_read, it * NUNIT + n + 1)
                            if b >= 2:
                                dve.wait_ge(split_done, it * NB + b - 1)
                            dve.tensor_reduce(negm[:, b % 2, :], mp[b % 2][:, :, 0:j + 1], AX.X, ALU.max, negate=True
                                              ).then_inc(negm_done, 1)
                    else:
                        dve.wait_ge(max_scored, it * NUNIT + n + 1)
                        if b >= 2:
                            uses, per = q_uses(b - 2)
                            dve.wait_ge(m_in[q_slot(b - 2)], 16 * GH * (it * per + uses + 1))
                        dve.tensor_copy(mrow[:, b % 2, :], bank[0:GH * NPART, :]).then_inc(max_read, 1)

                for unit in first:
                    do(unit)
                for st in plan:
                    for unit in st[4] + st[5]:
                        do(unit)

        @block.tensor
        def _(pe):
            pe.wait_ge(const_in, 5 * 16)
            pe.wait_ge(o_zero, 1)
            with pe.Fori(0, ITS) as it:
                seen_k = set()
                seen_q = set()

                def need_k(half, j):
                    for jj in range(j + 1):
                        if (half, jj) not in seen_k:
                            seen_k.add((half, jj))
                            pe.wait_ge(k_in[half][jj], 16 * 4 * (it + 1))

                def do(unit):
                    b = unit[1]
                    half, j = order[b]
                    n = unit_at[unit]
                    bank = ps_m[n % MR]
                    if n >= MR:
                        pe.wait_ge(max_read, it * NUNIT + n - MR + 1)
                    if unit[0] == "max":
                        _, _, a, h, cc = unit
                        if b not in seen_q:
                            seen_q.add(b)
                            uses, per = q_uses(b)
                            pe.wait_ge(q_in[q_slot(b)], 16 * len(Q_TERMS) * (it * per + uses + 1))
                        need_k(half, cc)
                        width = P * (a + 1) if cc == j else C
                        diag = cc == j
                        last = pe.matmul(bank[:, 0:width], qst[q_slot(b)][0:KQ, h, a * P:(a + 1) * P],
                                         kst[half][0:KQ, h, cc * C:cc * C + width], start=True, stop=True)
                        if diag:
                            last = pe.matmul(bank[:, a * P:width], id_b[:, :], mq_sb[:, :], start=False, stop=True,
                                             skip_group_check=True)
                        last.then_inc(max_scored, 1)
                    else:
                        pe.wait_ge(split_done, it * NB + b + 1)
                        for a in range(TPC):
                            last = pe.matmul(bank[0:GH * NPART, a * P:(a + 1) * P],
                                             msplit[:, b % 2, a * GH:(a + 1) * GH, :].rearrange("p h t -> p (h t)"),
                                             id_b[:, :], start=True, stop=True)
                        last.then_inc(max_scored, 1)

                def score(s, hp):
                    b, half, j, i, _, _ = plan[s]
                    off = max(0, i - TPC * j) * P
                    if i == 0 and hp == 0:
                        uses, per = q_uses(b)
                        pe.wait_ge(m_in[q_slot(b)], 16 * GH * (it * per + uses + 1))
                        need_k(half, j)
                    if s >= 1:
                        pe.wait_ge(exp_done, it * (2 * NSTEP) + 2 * s + hp - 1)
                    diag = i >= TPC * j
                    for x in range(2):
                        h = 2 * hp + x
                        last = pe.matmul(ps_s[hp][:, x, off:C], kst[half][0:KM, h, i * P:(i + 1) * P],
                                         qst[q_slot(b)][0:KM, h, off:C], start=True, stop=True)
                        if diag:
                            last = pe.matmul(ps_s[hp][:, x, off:off + P], id_b[:, :], mk_sb[:, :], start=False, stop=True,
                                             skip_group_check=True)
                    last.then_inc(scored, 1)

                for unit in first:
                    do(unit)
                score(0, 0)
                score(0, 1)
                for s, (b, half, j, i, turn, new) in enumerate(plan):
                    units = turn + new
                    cut = (len(units) + 1) // 2
                    for unit in units[:cut]:
                        do(unit)
                    if s + 1 < NSTEP:
                        score(s + 1, 0)
                    for unit in units[cut:]:
                        do(unit)
                    if s + 1 < NSTEP:
                        score(s + 1, 1)
                    off = max(0, i - TPC * j) * P
                    if i == 0 and b > 0:
                        pe.wait_ge(o_done, it * NB + b)
                    pe.wait_ge(exp_done, it * (2 * NSTEP) + 2 * s + 2)
                    for h in range(GH):
                        last = pe.matmul(ps_o[32 * h:32 * h + DV, off:C], vst[half][:, i, h * DV:(h + 1) * DV],
                                         probs[:, s % PR, h, off:C], start=(i == 0), stop=(s == last_step[b]),
                                         tile_position=(0, 32 * h))
                    last.then_inc(pv_done, 1)


def project_out(nc, Y, o_raw, w_o, b_o, bcast):
    with ExitStack() as ctx:
        def sb(name, shape, dt=F32):
            return ctx.enter_context(nc.sbuf_tensor(name, shape, dt))

        sem = ctx.enter_context(semaphores(nc))

        wo_sb = sb("owo", [P, G, E])
        bo_sb = sb("obo", [P, E])
        sel = sb("osel", [P, P])
        raw = sb("oraw", [P, G, C])
        rec = sb("orec", [P, G, C])
        on = sb("oon", [P, G, C])
        ps_d = ctx.enter_context(nc.psum_tensor("ops_d", [P, G, C], F32))
        ps_y = ctx.enter_context(nc.psum_tensor("ops_y", [P, TPC, 512], F32))
        const_in = sem("o_const_in")
        raw_in = sem("o_raw_in")
        den_done = sem("o_den_done")
        rec_done = sem("o_rec_done")
        on_done = sem("o_on_done")
        y_done = sem("o_y_done")
        y_out = sem("o_y_out")
        block = ctx.enter_context(nc.Block())

        @block.sync
        def _(sp):
            sp.dma_start(wo_sb[:, :, :], w_o).then_inc(const_in, 16)
            sp.dma_start(bo_sb[:, :], b_o).then_inc(const_in, 16)
            sp.dma_start(sel[:, :], bcast).then_inc(const_in, 16)
            def chunk(c):
                upto(sp, on_done, c * G)
                sp.dma_start(raw[:, :, :], o_raw[:, bass.ds(c, 1), :, :].rearrange("g c p n -> p g (c n)")
                             ).then_inc(raw_in, 16)
            repeat(sp, NC, chunk)

        @block.tensor
        def _(pe):
            pe.wait_ge(const_in, 48)
            def chunk(c):
                pe.wait_ge(raw_in, 16 * c + 16)
                upto(pe, rec_done, c * G)
                for g in range(G):
                    pe.matmul(ps_d[:, g, :], sel[:, :], raw[:, g, :], start=True, stop=True).then_inc(den_done, 1)
                upto(pe, y_out, c * TPC)
                for a in range(TPC):
                    for g in range(G):
                        if a == 0:
                            pe.wait_ge(on_done, c * G + g + 1)
                        last = pe.matmul(ps_y[:, a, 0:E], on[:, g, a * P:(a + 1) * P], wo_sb[:, g, :],
                                         start=(g == 0), stop=(g == G - 1))
                    last.then_inc(y_done, 1)
            repeat(pe, NC, chunk)

        @block.vector
        def _(dve):
            dve.wait_ge(const_in, 48)
            def chunk(c):
                for g in range(G):
                    dve.wait_ge(den_done, c * G + g + 1)
                    dve.reciprocal(rec[:, g, :], ps_d[:, g, :]).then_inc(rec_done, 1)
                upto(dve, y_done, c * TPC)
                for g in range(G):
                    dve.wait_ge(rec_done, c * G + g + 1)
                    dve.tensor_tensor(on[:, g, :], raw[:, g, :], rec[:, g, :], ALU.mult).then_inc(on_done, 1)
                for a in range(TPC):
                    dve.wait_ge(y_done, c * TPC + a + 1)
                    dve.tensor_tensor(Y[:, bass.ds(c * TPC + a, 1), :].rearrange("p a e -> p (a e)"),
                                      ps_y[:, a, 0:E], bo_sb[:, :], ALU.add).then_inc(y_out, 1)
            repeat(dve, NC, chunk)


def product3(pe, out, a_hi, a_lo, b_hi, b_lo, start, stop):
    pe.matmul(out, a_hi, b_hi, start=start, stop=False)
    pe.matmul(out, a_hi, b_lo, start=False, stop=False)
    return pe.matmul(out, a_lo, b_hi, start=False, stop=stop)


def local_attention_layer(nc, layer, X, w_qkv, w_o, rope_tables, rope_scale, ident, window_masks):
    with ExitStack() as ctx:
        def sb(name, shape, dt=F32):
            return ctx.enter_context(nc.sbuf_tensor(f"a{layer}_{name}", shape, dt))

        sem = ctx.enter_context(semaphores(nc, f"a{layer}_"))

        def psum(name, shape):
            return ctx.enter_context(nc.psum_tensor(f"a{layer}_{name}", shape, F32))

        OC = INNER // P
        stage = sb("stage", [P, EC * 3 * INNER])
        wq_hi, wq_lo = (sb(f"wq{i}", [P, EC, 3 * INNER], F32R) for i in "hl")
        wo_hi, wo_lo = (sb(f"wo{i}", [P, OC, E], F32R) for i in "hl")
        id_sb = sb("id", [P, P])
        masks = sb("masks", [P, 2, 2 * P])
        scale_sb = sb("scale", [P, 2, 2, LD])
        half = sb("half", [P, 2 * LH])
        xw = sb("xw", [P, 2, E])
        hT_hi, hT_lo = (sb(f"hT{i}", [P, 2, EC, P + 1], F32R) for i in "hl")
        qk = sb("qk", [P, 2, INNER])
        sq = sb("sq", [P, 2 * LH, LD])
        ss = sb("ss", [P, 2 * LH])
        ssc = sb("ssc", [P, 2 * LH])
        rn = sb("rn", [P, 2, 2 * LH])
        tab = sb("tab", [P, 2, 2, 2, LD])
        tabs = sb("tabs", [P, 2, 2, LD])
        t1 = sb("t1", [P, 2, INNER])
        t2 = sb("t2", [P, 2, INNER])
        ropes = sb("ropes", [P, 2, INNER])
        qkn = sb("qkn", [P, 2, INNER])
        qz = sb("qz", [P, 2, OC, P])
        kT = sb("kT", [P, 2, OC, P])
        V = sb("V", [P, 4, INNER])
        sc = sb("sc", [P, LH, 2 * P])
        mx = sb("mx", [P, LH])
        idle = sb("idle", [P, LH])
        nm = sb("nm", [P, LH])
        prob = sb("prob", [P, 2, LH, 2 * P])
        psm = sb("psm", [P, 2, LH])
        pinv = sb("pinv", [P, LH])
        PT = sb("PT", [P, 2 * LH, P])
        on = sb("on", [P, INNER])
        oT_hi, oT_lo = (sb(f"oT{i}", [P, OC, P], F32R) for i in "hl")

        bank_x = psum("bank_x", [P, 512])
        bank_s = [psum(f"bank_s{i}", [P, 512]) for i in range(2)]
        bank_q = psum("bank_q", [P, 512])
        bank_k = psum("bank_k", [P, 512])
        bank_v = psum("bank_v", [P, 512])
        bank_qk = psum("bank_qk", [P, 2, 512])

        const_in, wq_in, wo_in = sem("const_in"), sem("wq_in"), sem("wo_in")
        wh_done, wl_done = sem("wh_done"), sem("wl_done")
        zero_set, half_set = sem("zero_set"), sem("half_set")
        tab_in = [sem(f"tab_in{i}") for i in range(2)]
        names = ("xw", "tx", "hth", "htl", "qkmm", "vmm", "sqd", "qkc", "vc", "ssd", "sscd", "rnd", "tabd",
                 "t1d", "t2d", "sumd", "qnd", "tq", "qzd", "kt", "scored", "masked", "nmd", "expd", "tp",
                 "pta", "ptd", "av", "inv", "ond", "to", "oth", "otl", "wod", "x2d")
        (xw_done, tx_done, hth_done, htl_done, qk_done, v_done, sq_done, qkc_done, vc_done, ss_done, ssc_done,
         rn_done, tab_done, t1_done, t2_done, sum_done, qn_done, tq_done, qz_done, kt_done, scored, masked,
         nm_done, exp_done, tp_done, pta_done, ptd_done, av_done, inv_done, on_done, to_done, oth_done,
         otl_done, wo_done, x2_done) = [sem(n) for n in names]

        def slots(eng, slot):
            for k in range(4):
                slot(k, k)
            with eng.Fori(1, NT // 4) as it:
                for u in range(4):
                    slot(it * 4 + u, u)
            for k in range(NT, NT + 2):
                slot(k, k % 4)

        def live(w):
            return not isinstance(w, int) or 0 <= w < NT

        block = ctx.enter_context(nc.Block())

        @block.sync
        def _(sp):
            sp.dma_start(stage[:, :], w_qkv).then_inc(wq_in, 16)
            for dst, src in ((id_sb[:, :], ident), (masks[:, :, :], window_masks), (scale_sb[:, :, :, :], rope_scale)):
                sp.dma_start(dst, src).then_inc(const_in, 16)
            sp.wait_ge(wh_done, 1)
            sp.wait_ge(wl_done, 1)
            sp.dma_start(stage[:, 0:OC * E], w_o).then_inc(wo_in, 16)

            def slot(k, u):
                if live(k):
                    upto(sp, tab_done, k - 1)
                    sp.dma_start(tab[:, u % 2, :, :, :], rope_tables[bass.ds(k, 1)].rearrange("w p a b d -> (w p) a b d")
                                 ).then_inc(tab_in[u % 2], 16)
            slots(sp, slot)

        @block.gpsimd
        def _(pool):
            pool.memset(half[:, :], -0.5).then_inc(half_set, 1)
            pool.wait_ge(half_set, 1)
            pool.wait_ge(const_in, 48)

            def slot(k, u):
                if live(k):
                    p = u % 2
                    flat = "p a b d -> p (a b d)"
                    pool.wait_ge(tab_in[p], (k - p) * 8 + 16)
                    upto(pool, t1_done, k)
                    upto(pool, t2_done, 2 * k)
                    pool.tensor_tensor(tabs[:, :, :, :].rearrange(flat), tab[:, p, :, :, :].rearrange(flat),
                                       scale_sb[:, :, :, :].rearrange(flat), ALU.mult).then_inc(tab_done, 1)
                    pool.wait_ge(tab_done, k + 1)
                    pool.wait_ge(qkc_done, k + 1)
                    upto(pool, sum_done, k)
                    qh = qk[:, :, :].rearrange("p q (h d) -> p q h d", d=LD)
                    th = t2[:, :, :].rearrange("p q (h d) -> p q h d", d=LD)
                    HD = LD // 2
                    for lo, src in ((0, HD), (HD, 0)):
                        tb = tabs[:, 1, :, lo:lo + HD].rearrange("p q (o d) -> p q o d", o=1).broadcast_to([P, 2, LH, HD])
                        pool.tensor_tensor(th[:, :, :, lo:lo + HD], qh[:, :, :, src:src + HD], tb, ALU.mult
                                           ).then_inc(t2_done, 1)
                    pool.wait_ge(ssc_done, k + 1)
                    upto(pool, qn_done, k - 1)
                    pool.tensor_tensor(rn[:, p, :], ssc[:, :], half[:, :], ALU.pow).then_inc(rn_done, 1)
                    pool.wait_ge(t1_done, k + 1)
                    pool.wait_ge(t2_done, 2 * k + 2)
                    upto(pool, qn_done, k)
                    pool.tensor_tensor(ropes[:, :, :], t1[:, :, :], t2[:, :, :], ALU.add).then_inc(sum_done, 1)
            slots(pool, slot)

        @block.scalar
        def _(act):
            act.wait_ge(wq_in, 16)
            act.activation(wq_hi[:, :, :].rearrange("p a b -> p (a b)"), stage[:, :], ACT.Copy).then_inc(wh_done, 1)
            act.wait_ge(wo_in, 16)
            act.activation(wo_hi[:, :, :].rearrange("p a b -> p (a b)"), stage[:, 0:OC * E], ACT.Copy).then_inc(wh_done, 1)
            act.wait_ge(zero_set, 6)

            def slot(k, u):
                w, p = k - 2, u % 2
                if live(w):
                    upto(act, av_done, w)
                    for i in range(2):
                        act.wait_ge(tp_done, 4 * w + 2 * i + 1)
                        act.activation(PT[:, 8 * i:8 * i + 4, :], bank_s[0][:, :], ACT.Copy).then_inc(pta_done, 1)
                if live(k):
                    act.wait_ge(tx_done, k + 1)
                    upto(act, v_done, k - 1)
                    upto(act, hth_done, 2 * k)
                    act.activation(hT_hi[:, p, 1, 0:1], hT_hi[:, 1 - p, 1, P:P + 1].bitcast(F32), ACT.Copy).then_inc(hth_done, 1)
                    act.activation(hT_hi[:, p, :, 1:P + 1], bank_x[:, 0:E], ACT.Copy).then_inc(hth_done, 1)
                w = k - 1
                if live(w):
                    act.wait_ge(tq_done, 2 * w + 1)
                    upto(act, scored, 4 * w)
                    for i in range(2):
                        rows = slice(i * LD, i * LD + LD)
                        act.activation(qz[rows, i, :, :], bank_q[rows, :], ACT.Copy).then_inc(qz_done, 1)
                w = k - 2
                if live(w):
                    act.wait_ge(to_done, w + 1)
                    upto(act, wo_done, w)
                    act.activation(oT_hi[:, :, :], bank_x[:, :], ACT.Copy).then_inc(oth_done, 1)
                w = k - 1
                if live(w):
                    q = (u - 1) % 2
                    act.wait_ge(nm_done, w + 1)
                    upto(act, tp_done, 4 * (w - 1))
                    upto(act, on_done, w - 1)
                    for h in range(LH):
                        act.activation(prob[:, q, h, :], sc[:, h, :], ACT.Exp, bias=nm[:, h:h + 1],
                                       accum_out=psm[:, q, h:h + 1]).then_inc(exp_done, 1)
                if live(k):
                    act.wait_ge(qk_done, k + 1)
                    upto(act, ss_done, k)
                    act.activation(sq[:, :, :], bank_qk[:, :, :], ACT.Square).then_inc(sq_done, 1)
                    upto(act, t1_done, k)
                    upto(act, t2_done, 2 * k)
                    act.activation(qk[:, :, :], bank_qk[:, :, :], ACT.Copy).then_inc(qkc_done, 1)
                    act.wait_ge(v_done, k + 1)
                    upto(act, av_done, k - 2)
                    act.activation(V[:, u, :], bank_v[:, :], ACT.Copy).then_inc(vc_done, 1)
            slots(act, slot)

        @block.tensor
        def _(pe):
            pe.wait_ge(const_in, 48)
            pe.wait_ge(wh_done, 2)
            pe.wait_ge(wl_done, 2)
            pe.wait_ge(zero_set, 6)

            def slot(k, u):
                w = k - 2
                if live(w):
                    q = (u - 2) % 2
                    pe.wait_ge(exp_done, LH * (w + 1))
                    for i in range(4):
                        if i >= 2:
                            pe.wait_ge((pta_done, ptd_done)[i % 2], 2 * w + 1)
                        for j in range(4):
                            h, side = (4 * i + j) // 2, j % 2
                            last = pe.transpose(bank_s[i % 2][:, j * P:(j + 1) * P], prob[:, q, h, side * P:(side + 1) * P],
                                                id_sb[:, :])
                        last.then_inc(tp_done, 1)
                if live(k):
                    pe.wait_ge(xw_done, k + 1)
                    upto(pe, oth_done, k - 2)
                    upto(pe, otl_done, k - 2)
                    for e in range(EC):
                        last = pe.transpose(bank_x[:, e * P:(e + 1) * P], xw[:, u % 2, e * P:(e + 1) * P], id_sb[:, :])
                    last.then_inc(tx_done, 1)
                w = k - 1
                if live(w):
                    pe.wait_ge(qn_done, w + 1)
                    upto(pe, x2_done, w - 1)
                    upto(pe, kt_done, w)
                    for i, bank in enumerate((bank_q, bank_k)):
                        for j in range(OC):
                            last = pe.transpose(bank[:, j * P:(j + 1) * P], qkn[:, i, j * P:(j + 1) * P], id_sb[:, :])
                        last.then_inc(tq_done, 1)
                w = k - 2
                if live(w):
                    pe.wait_ge(pta_done, 2 * w + 2)
                    pe.wait_ge(ptd_done, 2 * w + 2)
                    upto(pe, vc_done, (w + 2) if not isinstance(w, int) else min(w + 2, NT))
                    for h in range(LH):
                        for side in range(2):
                            last = pe.matmul(bank_v[:, h * LD:(h + 1) * LD], PT[:, 2 * h + side, :],
                                             V[:, (u - 3 + side) % 4, h * LD:(h + 1) * LD],
                                             start=(side == 0), stop=(side == 1))
                    last.then_inc(av_done, 1)
                w = k - 1
                if live(w):
                    q = (u - 1) % 2
                    pe.wait_ge(qz_done, 2 * w + 2)
                    pe.wait_ge(kt_done, w + 1)
                    for i in range(4):
                        if i >= 2:
                            pe.wait_ge(masked, LH * w + 2 * (i - 1))
                        for j in range(2):
                            h = 2 * i + j
                            for side in range(2):
                                last = pe.matmul(bank_s[i % 2][:, (2 * j + side) * P:(2 * j + side + 1) * P],
                                                 qz[:, h % 2, h // 2, :], kT[:, q if side else 1 - q, h // 2, :],
                                                 start=True, stop=True)
                        last.then_inc(scored, 1)
                w = k - 2
                if live(w):
                    pe.wait_ge(on_done, w + 1)
                    upto(pe, hth_done, 2 * (k + 1) if not isinstance(k, int) else 2 * min(k + 1, NT))
                    upto(pe, htl_done, 2 * (k + 1) if not isinstance(k, int) else 2 * min(k + 1, NT))
                    for j in range(OC):
                        last = pe.transpose(bank_x[:, j * P:(j + 1) * P], on[:, j * P:(j + 1) * P], id_sb[:, :])
                    last.then_inc(to_done, 1)
                if live(k):
                    pe.wait_ge(hth_done, 2 * k + 2)
                    pe.wait_ge(htl_done, 2 * k + 2)
                    upto(pe, sq_done, k)
                    upto(pe, qkc_done, k)
                    upto(pe, on_done, k - 1)
                    p = u % 2
                    for n in range(3):
                        dst = bank_qk[:, n, :] if n < 2 else bank_v[:, :]
                        cols = slice(n * INNER, (n + 1) * INNER)
                        for e in range(EC):
                            tok = slice(1 - e, 1 - e + P)
                            last = product3(pe, dst, hT_hi[:, p, e, tok], hT_lo[:, p, e, tok], wq_hi[:, e, cols],
                                            wq_lo[:, e, cols], e == 0, e == EC - 1)
                        if n >= 1:
                            last.then_inc((qk_done, v_done)[n - 1], 1)
                w = k - 2
                if live(w):
                    pe.wait_ge(oth_done, w + 1)
                    pe.wait_ge(otl_done, w + 1)
                    upto(pe, qz_done, 2 * (w + 2) if not isinstance(w, int) else 2 * min(w + 2, NT))
                    for j in range(OC):
                        last = product3(pe, bank_q[:, 0:E], oT_hi[:, j, :], oT_lo[:, j, :], wo_hi[:, j, :], wo_lo[:, j, :],
                                        j == 0, j == OC - 1)
                    last.then_inc(wo_done, 1)
            slots(pe, slot)

        @block.vector
        def _(dve):
            dve.memset(hT_hi[:, 1, 1, P:P + 1].bitcast(F32), 0.0).then_inc(zero_set, 1)
            dve.memset(hT_lo[:, 1, 1, P:P + 1].bitcast(F32), 0.0).then_inc(zero_set, 1)
            dve.memset(kT[:, 1, :, :], 0.0).then_inc(zero_set, 1)
            dve.memset(V[:, 3, :], 0.0).then_inc(zero_set, 1)
            dve.memset(qz[0:LD, 1, :, :], 0.0).then_inc(zero_set, 1)
            dve.memset(qz[LD:P, 0, :, :], 0.0).then_inc(zero_set, 1)
            dve.wait_ge(wh_done, 1)
            dve.tensor_tensor(wq_lo[:, :, :].rearrange("p a b -> p (a b)"), stage[:, :],
                              wq_hi[:, :, :].rearrange("p a b -> p (a b)").bitcast(F32), ALU.subtract).then_inc(wl_done, 1)
            dve.wait_ge(wh_done, 2)
            dve.tensor_tensor(wo_lo[:, :, :].rearrange("p a b -> p (a b)"), stage[:, 0:OC * E],
                              wo_hi[:, :, :].rearrange("p a b -> p (a b)").bitcast(F32), ALU.subtract).then_inc(wl_done, 1)
            dve.wait_ge(const_in, 48)
            dve.wait_ge(zero_set, 6)

            def slot(k, u):
                w = k - 2
                if live(k):
                    upto(dve, tx_done, k - 1)
                    dve.tensor_copy(xw[:, u % 2, :], X[:, bass.ds(k, 1), :].rearrange("p a e -> p (a e)")).then_inc(xw_done, 1)
                if live(w):
                    upto(dve, av_done, w)
                    for i in range(2):
                        dve.wait_ge(tp_done, 4 * w + 2 * i + 2)
                        dve.tensor_copy(PT[:, 8 * i + 4:8 * i + 8, :].rearrange("p a b -> p (a b)"), bank_s[1][:, :]
                                        ).then_inc(ptd_done, 1)
                w = k - 1
                if live(w):
                    q = (u - 1) % 2
                    dve.wait_ge(sum_done, w + 1)
                    dve.wait_ge(rn_done, w + 1)
                    upto(dve, tq_done, 2 * w)
                    dve.tensor_tensor(qkn[:, :, :].rearrange("p q (h d) -> p (q h) d", d=LD),
                                      ropes[:, :, :].rearrange("p q (h d) -> p (q h) d", d=LD),
                                      rn[:, q, :].rearrange("p (h o) -> p h o", o=1).broadcast_to([P, 2 * LH, LD]),
                                      ALU.mult).then_inc(qn_done, 1)
                if live(k):
                    p = u % 2
                    dve.wait_ge(hth_done, 2 * k + 2)
                    upto(dve, htl_done, 2 * k)
                    upto(dve, v_done, k - 1)
                    dve.tensor_copy(hT_lo[:, p, 1, 0:1], hT_lo[:, 1 - p, 1, P:P + 1].bitcast(F32)).then_inc(htl_done, 1)
                    dve.tensor_tensor(hT_lo[:, p, :, 1:P + 1], bank_x[:, 0:E].rearrange("p (e t) -> p e t", e=EC),
                                      hT_hi[:, p, :, 1:P + 1].bitcast(F32), ALU.subtract).then_inc(htl_done, 1)
                w = k - 1
                if live(w):
                    q = (u - 1) % 2
                    dve.wait_ge(tq_done, 2 * w + 2)
                    upto(dve, scored, 4 * w)
                    dve.tensor_copy(kT[:, q, :, :].rearrange("p a b -> p (a b)"), bank_k[:, :]).then_inc(kt_done, 1)
                w = k - 2
                if live(w):
                    q = (u - 2) % 2
                    dve.reciprocal(pinv[:, :], psm[:, q, :]).then_inc(inv_done, 1)
                    dve.wait_ge(inv_done, w + 1)
                    dve.wait_ge(av_done, w + 1)
                    upto(dve, to_done, w)
                    dve.tensor_tensor(on[:, :].rearrange("p (h d) -> p h d", d=LD),
                                      bank_v[:, :].rearrange("p (h d) -> p h d", d=LD),
                                      pinv[:, :].rearrange("p (h o) -> p h o", o=1).broadcast_to([P, LH, LD]),
                                      ALU.mult).then_inc(on_done, 1)
                w = k - 1
                if live(w):
                    mask = masks[:, 0 if isinstance(w, int) and w == 0 else 1, :]
                    upto(dve, exp_done, LH * w)
                    for h in range(LH):
                        if h % 2 == 0:
                            dve.wait_ge(scored, 4 * w + h // 2 + 1)
                            dve.memset(idle[:, h:h + 1], 0.0)
                        dve.tensor_tensor_reduce(sc[:, h, :], bank_s[(h // 2) % 2][:, (h % 2) * 2 * P:(h % 2 + 1) * 2 * P],
                                                 mask, 1.0, -3.0e38, ALU.add, ALU.max, mx[:, h:h + 1]).then_inc(masked, 1)
                    dve.wait_ge(masked, LH * (w + 1))
                    dve.tensor_scalar(nm[:, :], mx[:, :], -1.0, None, ALU.mult).then_inc(nm_done, 1)
                w = k - 2
                if live(w):
                    dve.wait_ge(oth_done, w + 1)
                    dve.tensor_tensor(oT_lo[:, :, :].rearrange("p a b -> p (a b)"), bank_x[:, :],
                                      oT_hi[:, :, :].rearrange("p a b -> p (a b)").bitcast(F32), ALU.subtract
                                      ).then_inc(otl_done, 1)
                if live(k):
                    dve.wait_ge(sq_done, k + 1)
                    dve.tensor_reduce(ss[:, :], sq[:, :, :], AX.X, ALU.add).then_inc(ss_done, 1)
                    dve.wait_ge(ss_done, k + 1)
                    upto(dve, rn_done, k)
                    dve.tensor_scalar(ssc[:, :], ss[:, :], 1e-24, None, ALU.max).then_inc(ssc_done, 1)
                    dve.wait_ge(qkc_done, k + 1)
                    dve.wait_ge(tab_done, k + 1)
                    upto(dve, sum_done, k)
                    dve.tensor_tensor(t1[:, :, :].rearrange("p q (h d) -> p q h d", d=LD),
                                      qk[:, :, :].rearrange("p q (h d) -> p q h d", d=LD),
                                      tabs[:, 0, :, :].rearrange("p q (o d) -> p q o d", o=1).broadcast_to([P, 2, LH, LD]),
                                      ALU.mult).then_inc(t1_done, 1)
                w = k - 2
                if live(w):
                    dve.wait_ge(wo_done, w + 1)
                    xt = X[:, bass.ds(w, 1), :].rearrange("p a e -> p (a e)")
                    dve.tensor_tensor(xt, bank_q[:, 0:E], xt, ALU.add).then_inc(x2_done, 1)
            slots(dve, slot)


def mlp_layer(nc, layer, X, w_1, w_2, b_1, ln_cols, b_2, ident, shift, carry):
    with ExitStack() as ctx:
        def sb(name, shape, dt=F32):
            return ctx.enter_context(nc.sbuf_tensor(f"m{layer}_{name}", shape, dt))

        sem = ctx.enter_context(semaphores(nc, f"m{layer}_"))

        def psum(name, shape):
            return ctx.enter_context(nc.psum_tensor(f"m{layer}_{name}", shape, F32))

        stage = sb("stage", [P, EC * 2 * HP])
        w1_hi, w1_lo = (sb(f"w1{i}", [P, EC, 2 * HP], F32R) for i in "hl")
        w2_hi, w2_lo = (sb(f"w2{i}", [P, HC, E], F32R) for i in "hl")
        b1_sb = sb("b1", [P, 2 * HC])
        ln_sb = sb("ln", [P, 2 * EC])
        b2_sb = sb("b2", [P, E])
        id_sb = sb("id", [P, P])
        sh_sb = sb("sh", [P, P])
        ca_sb = sb("ca", [P, P])
        half = sb("half", [P, TPC])
        stats = sb("stats", [P, TPC, 2, 6])
        mv = sb("mv", [P, TPC, 2])
        idle = sb("idle", [P, 1])
        ve = sb("ve", [P, TPC])
        rstd = sb("rstd", [P, TPC])
        hn = sb("hn", [P, TPC, E])
        hf = sb("hf", [P, EC, C])
        h_hi, h_lo = (sb(f"h{i}", [P, EC, C], F32R) for i in "hl")
        gl = sb("gl", [P, 2, C])
        uf = sb("uf", [P, 2, C])
        u_hi, u_lo = (sb(f"u{i}", [P, HC, C], F32R) for i in "hl")
        xb = sb("xb", [P, TPC, E])
        bank_sh = psum("bank_sh", [P, TPC, P])
        bank_t = psum("bank_t", [P, EC, C])
        UR = 3
        bank_u = [psum(f"bank_u{i}", [P, C]) for i in range(UR)]
        bank_y = psum("bank_y", [P, TPC, E])

        const_in, w1_in, w2_in = sem("const_in"), sem("w1_in"), sem("w2_in")
        wh_done, wl_done, half_set = sem("wh_done"), sem("wl_done"), sem("half_set")
        names = ("sh", "st", "ag", "ve", "rs", "hn", "th", "hf", "hhi", "hlo", "um", "gl", "uf", "uh", "ul", "y", "xb", "x3")
        (sh_done, st_done, ag_done, ve_done, rs_done, hn_done, th_done, hf_done, hhi_done, hlo_done, um_done,
         gl_done, uf_done, uh_done, ul_done, y_done, xb_done, x3_done) = [sem(n) for n in names]

        def slots(eng, slot):
            slot(0)
            with eng.Fori(1, NC) as k:
                slot(k)
            slot(NC)

        def live(c):
            return not isinstance(c, int) or 0 <= c < NC

        def tile(k, a):
            return X[:, bass.ds(k * TPC + a, 1), :]

        block = ctx.enter_context(nc.Block())

        @block.sync
        def _(sp):
            sp.dma_start(stage[:, :], w_1).then_inc(w1_in, 16)
            for dst, src in ((b1_sb, b_1), (ln_sb, ln_cols), (b2_sb, b_2), (id_sb, ident), (sh_sb, shift), (ca_sb, carry)):
                sp.dma_start(dst[:, :], src).then_inc(const_in, 16)
            sp.wait_ge(wh_done, 1)
            sp.wait_ge(wl_done, 1)
            sp.dma_start(stage[:, 0:HC * E], w_2).then_inc(w2_in, 16)

        @block.gpsimd
        def _(pool):
            pool.memset(half[:, :], -0.5).then_inc(half_set, 1)
            pool.wait_ge(half_set, 1)

            def slot(k):
                if live(k):
                    pool.wait_ge(ve_done, k + 1)
                    upto(pool, hn_done, 2 * TPC * k)
                    pool.tensor_tensor(rstd[:, :], ve[:, :], half[:, :], ALU.pow).then_inc(rs_done, 1)
                if live(k - 1):
                    c = k - 1
                    for m in range(HC):
                        pool.wait_ge(uh_done, c * HC + m + 1)
                        if m == 0:
                            upto(pool, y_done, c)
                        pool.tensor_tensor(u_lo[:, m, :], uf[:, m % 2, :], u_hi[:, m, :].bitcast(F32), ALU.subtract
                                           ).then_inc(ul_done, 1)
            slots(pool, slot)

        @block.scalar
        def _(act):
            act.wait_ge(w1_in, 16)
            act.activation(w1_hi[:, :, :].rearrange("p a b -> p (a b)"), stage[:, :], ACT.Copy).then_inc(wh_done, 1)
            act.wait_ge(w2_in, 16)
            act.activation(w2_hi[:, :, :].rearrange("p a b -> p (a b)"), stage[:, 0:HC * E], ACT.Copy).then_inc(wh_done, 1)
            act.wait_ge(const_in, 6 * 16)

            def slot(k):
                if live(k - 1):
                    c = k - 1
                    for m in range(HC):
                        act.wait_ge(um_done, 2 * (c * HC + m) + 1)
                        if m >= 2:
                            act.wait_ge(uf_done, c * HC + m - 1)
                        else:
                            upto(act, uf_done, c * HC)
                        act.activation(gl[:, m % 2, :], bank_u[(2 * m) % UR][:, :], ACT.Gelu,
                                       bias=b1_sb[:, HC + m:HC + m + 1]).then_inc(gl_done, 1)
                if live(k):
                    for e in range(EC):
                        act.wait_ge(th_done, k * EC + e + 1)
                        upto(act, hlo_done, k * EC)
                        act.activation(hf[:, e, :], bank_t[:, e, :], ACT.Identity, scale=ln_sb[:, e:e + 1],
                                       bias=ln_sb[:, EC + e:EC + e + 1]).then_inc(hf_done, 1)
            slots(act, slot)

        @block.tensor
        def _(pe):
            pe.wait_ge(const_in, 6 * 16)
            pe.wait_ge(wh_done, 2)
            pe.wait_ge(wl_done, 2)

            def slot(k):
                if live(k):
                    upto(pe, hn_done, 2 * TPC * k)
                    for a in range(TPC):
                        first = isinstance(k, int) and k == 0 and a == 0
                        last = pe.matmul(bank_sh[:, a, :], sh_sb[:, :], tile(k, a)[:, :, P:E], start=True, stop=first)
                        if not first:
                            last = pe.matmul(bank_sh[:, a, :], ca_sb[:, :], tile(k, a - 1)[:, :, P:E], start=False, stop=True)
                    last.then_inc(sh_done, 1)
                c = k - 1
                if live(c):
                    pe.wait_ge(hlo_done, c * EC + EC)
                    pe.wait_ge(hhi_done, c * EC + EC)
                    for m in range(HC):
                        for side in range(2):
                            n = 2 * m + side
                            if n >= UR:
                                mm, ss = (n - UR) // 2, (n - UR) % 2
                                pe.wait_ge(uf_done if ss else gl_done, c * HC + mm + 1)
                            elif n == 0:
                                upto(pe, uf_done, c * HC)
                                upto(pe, gl_done, c * HC)
                            col = (HP if side == 0 else 0) + m * P
                            for e in range(EC):
                                last = product3(pe, bank_u[n % UR][:, :], w1_hi[:, e, col:col + P], w1_lo[:, e, col:col + P],
                                                h_hi[:, e, :], h_lo[:, e, :], e == 0, e == EC - 1)
                            last.then_inc(um_done, 1)
                if live(k):
                    pe.wait_ge(hn_done, 2 * TPC * (k + 1))
                    upto(pe, hf_done, k * EC)
                    for e in range(EC):
                        for a in range(TPC):
                            last = pe.transpose(bank_t[:, e, a * P:(a + 1) * P], hn[:, a, e * P:(e + 1) * P], id_sb[:, :])
                        last.then_inc(th_done, 1)
                if live(c):
                    upto(pe, x3_done, c * TPC)
                    for a in range(TPC):
                        for m in range(HC):
                            if a == 0:
                                pe.wait_ge(ul_done, c * HC + m + 1)
                            tok = slice(a * P, (a + 1) * P)
                            last = product3(pe, bank_y[:, a, :], u_hi[:, m, tok], u_lo[:, m, tok], w2_hi[:, m, :],
                                            w2_lo[:, m, :], m == 0, m == HC - 1)
                        if a == TPC - 1:
                            last.then_inc(y_done, 1)
            slots(pe, slot)

        @block.vector
        def _(dve):
            for i, (hi, lo, s, n) in enumerate(((w1_hi, w1_lo, w1_in, EC * 2 * HP), (w2_hi, w2_lo, w2_in, HC * E))):
                dve.wait_ge(wh_done, i + 1)
                dve.tensor_tensor(lo[:, :, :].rearrange("p a b -> p (a b)"), stage[:, 0:n],
                                  hi[:, :, :].rearrange("p a b -> p (a b)").bitcast(F32), ALU.subtract).then_inc(wl_done, 1)
            dve.wait_ge(const_in, 6 * 16)

            def slot(k):
                c = k - 1
                if live(k):
                    for a in range(TPC):
                        dve.bn_stats(stats[:, a, 0, :], tile(k, a)[:, :, 0:P].rearrange("p a e -> p (a e)")).then_inc(st_done, 1)
                    dve.wait_ge(sh_done, k + 1)
                    for a in range(TPC):
                        dve.bn_stats(stats[:, a, 1, :], bank_sh[:, a, :]).then_inc(st_done, 1)
                    dve.wait_ge(st_done, 2 * TPC * (k + 1))
                    dve.memset(idle[:, :], 0.0)
                    for a in range(TPC):
                        dve.bn_aggr(mv[:, a, :], stats[:, a, :, :]).then_inc(ag_done, 1)
                    dve.wait_ge(ag_done, TPC * (k + 1))
                    dve.tensor_scalar(ve[:, :], mv[:, :, 1], EPS, None, ALU.add).then_inc(ve_done, 1)
                    dve.wait_ge(rs_done, k + 1)
                    upto(dve, th_done, k * EC)
                    for a in range(TPC):
                        dve.tensor_scalar(hn[:, a, 0:P], tile(k, a)[:, :, 0:P].rearrange("p a e -> p (a e)"), mv[:, a, 0:1],
                                          rstd[:, a:a + 1], ALU.subtract, ALU.mult).then_inc(hn_done, 1)
                        dve.tensor_scalar(hn[:, a, P:E], bank_sh[:, a, :], mv[:, a, 0:1],
                                          rstd[:, a:a + 1], ALU.subtract, ALU.mult).then_inc(hn_done, 1)
                if live(c):
                    upto(dve, x3_done, c * TPC)
                    for a in range(TPC):
                        dve.tensor_tensor(xb[:, a, :], tile(c, a).rearrange("p a e -> p (a e)"), b2_sb[:, :], ALU.add
                                          ).then_inc(xb_done, 1)
                    for m in range(HC):
                        n = c * HC + m
                        dve.wait_ge(um_done, 2 * n + 2)
                        dve.wait_ge(gl_done, n + 1)
                        if m >= 2:
                            dve.wait_ge(ul_done, n - 1)
                        else:
                            upto(dve, ul_done, c * HC)
                        dve.scalar_tensor_tensor(out=uf[:, m % 2, :], in0=bank_u[(2 * m + 1) % UR][:, :],
                                                 scalar=b1_sb[:, m:m + 1], in1=gl[:, m % 2, :], op0=ALU.add, op1=ALU.mult
                                                 ).then_inc(uf_done, 1)
                        dve.wait_ge(uf_done, n + 1)
                        if m == 0:
                            upto(dve, y_done, c)
                        dve.tensor_copy(u_hi[:, m, :], uf[:, m % 2, :]).then_inc(uh_done, 1)
                if live(k):
                    for e in range(EC):
                        dve.wait_ge(hf_done, k * EC + e + 1)
                        if e == 0:
                            upto(dve, um_done, 2 * HC * k)
                        dve.tensor_copy(h_hi[:, e, :], hf[:, e, :]).then_inc(hhi_done, 1)
                    for e in range(EC):
                        dve.wait_ge(hhi_done, k * EC + e + 1)
                        dve.tensor_tensor(h_lo[:, e, :], hf[:, e, :], h_hi[:, e, :].bitcast(F32), ALU.subtract
                                          ).then_inc(hlo_done, 1)
                if live(c):
                    dve.wait_ge(y_done, c + 1)
                    dve.wait_ge(xb_done, TPC * (c + 1))
                    upto(dve, sh_done, (k + 1) if not isinstance(k, int) else min(k + 1, NC))
                    for a in range(TPC):
                        dve.tensor_tensor(tile(c, a).rearrange("p a e -> p (a e)"), bank_y[:, a, :], xb[:, a, :], ALU.add
                                          ).then_inc(x3_done, 1)
            slots(dve, slot)


def gate(nc, X, Y, x, out):
    with ExitStack() as ctx:
        x0 = ctx.enter_context(nc.sbuf_tensor("f_x0", [P, NT, E], F32))
        sg = ctx.enter_context(nc.sbuf_tensor("f_sg", [P, NT, E], F32))
        pr = ctx.enter_context(nc.sbuf_tensor("f_pr", [P, NT, E], F32))
        sem = ctx.enter_context(semaphores(nc))
        x_in = [sem(f"f_x_in{i}") for i in range(NC)]
        silu_done, prod_done, sum_done, stored = (sem(f"f_{n}") for n in ("silu", "prod", "sum", "stored"))
        block = ctx.enter_context(nc.Block())

        def part(t, c):
            return t[:, c * TPC:(c + 1) * TPC, :]

        def rows(d, c):
            return d[c * C:(c + 1) * C, :].rearrange("(a p) e -> p a e", p=P)

        @block.sync
        def _(sp):
            for c in range(NC):
                sp.dma_start(part(x0, c), rows(x, c)).then_inc(x_in[c], 16)
            for c in range(NC):
                sp.wait_ge(sum_done, c + 1)
                sp.dma_start(rows(out, c), part(pr, c)).then_inc(stored, 16)
            sp.wait_ge(stored, 16 * NC)

        @block.scalar
        def _(act):
            for c in range(NC):
                act.activation(part(sg, c), part(X, c), ACT.Silu).then_inc(silu_done, 1)

        @block.vector
        def _(dve):
            for c in range(NC):
                dve.wait_ge(silu_done, c + 1)
                dve.tensor_tensor(part(sg, c), part(Y, c), part(sg, c), ALU.mult).then_inc(prod_done, 1)
                dve.wait_ge(prod_done, c + 1)
                dve.wait_ge(x_in[c], 16)
                dve.tensor_tensor(part(pr, c), part(sg, c), part(x0, c), ALU.add).then_inc(sum_done, 1)


def build(nc, t, out, stop=99):
    X = nc.alloc_sbuf_tensor("X", [P, NT, E], F32)
    Y = nc.alloc_sbuf_tensor("Y", [P, NT, E], F32)
    k_parts = nc.dram_tensor("k_parts", [H, NPART, D, S], BF16).ap()
    q_parts = nc.dram_tensor("q_parts", [H, NPART, D, S], BF16).ap()
    v_aug = nc.dram_tensor("v_aug", [G, P, NT, GH * DV], F32).ap()
    o_raw = nc.dram_tensor("o_raw", [G, NC, P, C], F32).ap()
    layer_norm_and_project(nc, None, X, t["x"], t["w_qkv"], t["b_cols"], t["b_v"], t["cos"], t["sin"], t["ident"],
                           k_parts, q_parts, v_aug)
    global_attention(nc, k_parts, q_parts, v_aug, o_raw, *(t[n].bitcast(BF16) for n in ("identb", "mask_k", "mask_q", "ones")))
    project_out(nc, Y, o_raw, t["w_o"], t["b_o"], t["bcast"])
    for layer in range(DEPTH):
        n = str(layer)
        local_attention_layer(nc, layer, X, t["w_lqkv" + n], t["w_lo" + n], t["rope"], t["rope_scale" + n], t["ident"],
                              t["window_masks"])
        mlp_layer(nc, layer, X, t["w_1" + n], t["w_2" + n], t["b_1" + n], t["ln" + n], t["b_2" + n], t["ident"],
                  t["shift"], t["carry"])
    gate(nc, X, Y, t["x"], out)


def lay_out(inp):
    import numpy as np
    f = {k: np.asarray(v) for k, v in inp.items()}
    arr = {}

    def bf16_bits(w):
        return (w.astype(np.float32).view(np.uint32) >> 16).astype(np.uint16)

    def rows(w):
        return np.ascontiguousarray(w.reshape(-1, P, w.shape[1]).transpose(1, 0, 2))

    pair = np.arange(E).reshape(-1, 2)[:, ::-1].reshape(-1)
    wq, wk, wv = f["L0_attn_Wq"], f["L0_attn_Wk"], f["L0_attn_Wv"]
    bq, bk = f["L0_attn_bq"], f["L0_attn_bk"]
    arr["x"] = np.ascontiguousarray(f["L0_attn_x"].reshape(S, E))
    arr["w_qkv"] = rows(np.concatenate([wq.T, wq[pair].T, wk.T, wk[pair].T, wv.T], axis=1))
    arr["b_cols"] = np.ascontiguousarray(np.concatenate([b.reshape(EC, P) for b in (bq, bq[pair], bk, bk[pair])]).T)
    arr["b_v"] = np.ascontiguousarray(np.broadcast_to(f["L0_attn_bv"], (P, E)))
    inv = (1.0 / np.float32(10000.0) ** (np.arange(D // 2, dtype=np.float32) / (D // 2))).astype(np.float32)
    ang = (np.arange(S, dtype=np.float32)[:, None] * inv[None, :]).astype(np.float32).astype(np.float64)
    cos, sin = np.repeat(np.cos(ang), 2, axis=1), np.repeat(np.sin(ang), 2, axis=1)
    sin[:, 0::2] *= -1.0
    arr["cos"] = np.ascontiguousarray(np.tile(cos.T, (P // D, 1)).astype(np.float32))
    arr["sin"] = np.ascontiguousarray(np.tile(sin.T, (P // D, 1)).astype(np.float32))
    arr["ident"] = np.eye(P, dtype=np.float32)
    arr["identb"] = bf16_bits(np.eye(P))
    r, c = np.arange(P)[:, None], np.arange(P)[None, :]
    arr["mask_k"] = bf16_bits(np.where(r > c, MASKED, 0.0))
    arr["mask_q"] = bf16_bits(np.where(c > r, MASKED, 0.0))
    arr["ones"] = bf16_bits(np.ones((NPART, GH, S)))
    wo = np.zeros((P, G, E), np.float32)
    for g in range(G):
        for h in range(GH):
            for_rows = slice((g * GH + h) * D, (g * GH + h + 1) * D)
            wo[32 * h:32 * h + D, g, :] = f["L0_attn_Wo"][:, for_rows].T
    arr["w_o"] = wo
    arr["b_o"] = np.ascontiguousarray(np.broadcast_to(f["L0_attn_bo"], (P, E)))
    for l in range(DEPTH):
        n = str(l)
        arr["w_lqkv" + n] = rows(f["L0_ffn_wqkv"][l]).reshape(P, -1)
        arr["w_lo" + n] = rows(f["L0_ffn_wo"][l]).reshape(P, -1)
        qs, ks = f["L0_ffn_q_scale"][l], f["L0_ffn_k_scale"][l]
        turned = np.roll(np.arange(LD), LD // 2)
        scale = np.stack([np.stack([qs, ks]), np.stack([qs[turned], ks[turned]])])
        arr["rope_scale" + n] = np.ascontiguousarray(np.broadcast_to(scale, (P,) + scale.shape))
        w1, b1 = f["L0_ffn_w1"][l], f["L0_ffn_b1"][l]
        w1p, b1p = np.zeros((E, 2, HP), np.float32), np.zeros((2, HP), np.float32)
        w1p[:, :, :HID], b1p[:, :HID] = w1.reshape(E, 2, HID), b1.reshape(2, HID)
        arr["w_1" + n] = rows(w1p.reshape(E, 2 * HP)).reshape(P, -1)
        arr["b_1" + n] = np.ascontiguousarray(b1p.reshape(2 * HC, P).T)
        w2p = np.zeros((HP, E), np.float32)
        w2p[:HID] = f["L0_ffn_w2"][l]
        arr["w_2" + n] = rows(w2p).reshape(P, -1)
        arr["ln" + n] = np.ascontiguousarray(np.concatenate(
            [f["L0_ffn_ln_g"][l].reshape(EC, P), f["L0_ffn_ln_b"][l].reshape(EC, P)]).T)
        arr["b_2" + n] = np.ascontiguousarray(np.broadcast_to(f["L0_ffn_b2"][l], (P, E)))
    hd = np.arange(0, LD, 2, dtype=np.float32)
    freq = (np.arange(S, dtype=np.float32)[:, None] * (1.0 / np.float32(10000.0) ** (hd / LD)).astype(np.float32)[None, :])
    freq = np.concatenate([freq, freq], axis=1).astype(np.float64)
    base = (hd.astype(np.float64) + 0.4 * LD) / (1.4 * LD)
    grow = base[None, :] ** ((np.arange(S)[:, None] - S // 2) / (P / 2.0))
    grow = np.concatenate([grow, grow], axis=1)
    sign = np.where(np.arange(LD) < LD // 2, -1.0, 1.0)[None, :]
    table = np.stack([np.stack([8.0 * np.cos(freq) * grow, np.cos(freq) / grow], axis=1),
                      np.stack([8.0 * sign * np.sin(freq) * grow, sign * np.sin(freq) / grow], axis=1)], axis=1)
    arr["rope"] = np.ascontiguousarray(table.reshape(NT, P, 2, 2, LD).astype(np.float32))
    before = np.where(c < r, MASKED, 0.0)
    own = np.where(c > r, MASKED, 0.0)
    arr["window_masks"] = np.ascontiguousarray(np.stack(
        [np.concatenate([np.full((P, P), MASKED), own], 1), np.concatenate([before, own], 1)], 1).astype(np.float32))
    arr["shift"] = (c == r + 1).astype(np.float32)
    arr["carry"] = ((r == P - 1) & (c == 0)).astype(np.float32)
    arr["bcast"] = (r == 32 * (c // 32) + D).astype(np.float32)
    return arr


def kernel(**inputs):
    import concourse.bacc as bacc
    from concourse.bass_utils import run_bass_kernel_spmd
    arrays = lay_out(inputs)
    nc = bacc.Bacc("TRN2", target_bir_lowering=False, num_devices=1)
    t = {n: nc.dram_tensor("in_" + n, a.shape, mybir.dt.from_np(a.dtype), kind="ExternalInput").ap()
         for n, a in arrays.items()}
    out = nc.dram_tensor("out", (S, E), F32, kind="ExternalOutput").ap()
    build(nc, t, out)
    r = run_bass_kernel_spmd(nc, [{"in_" + n: a for n, a in arrays.items()}], core_ids=[0])
    return r.results[0]["out"].reshape(1, S, E)
```
